# Optimizing a Trainium2 kernel written in Bass

```python
import numpy as np
import jax
import jax.numpy as jnp

def _softmax(x, axis=-1):
    return jax.nn.softmax(x, axis=axis)
def _gelu(x):
    return jax.nn.gelu(x, approximate=True)
def _silu(x):
    return jax.nn.silu(x)
def _sigmoid(x):
    return jax.nn.sigmoid(x)
def _layernorm(x, axis=-1, eps=1e-5):
    m = jnp.mean(x, axis=axis, keepdims=True)
    v = jnp.var(x, axis=axis, keepdims=True)
    return (x - m) / jnp.sqrt(v + eps)
def _scatter_add(tgt, idx, src, axis=0):
    return tgt.at[idx].add(src)
def _segment_sum(src, seg, n):
    return jax.ops.segment_sum(src, seg, n)

kernel_name = 'mk_adj_resnorm_d1_adj_256_0024ed'

def setup_inputs(seed: int = 0):
    np.random.seed(seed)
    _w = jnp.asarray
    def _rec_inputs():
        import jax
        import jax.numpy as jnp
        _gk = jax.random.key(seed)
        x = -0.0002144 + 1 * jax.random.normal(jax.random.fold_in(_gk, 1), (16, 1024, 256), jnp.float32)
        _a = jax.random.bernoulli(jax.random.fold_in(_gk, 2), 0.03125, (16, 1024, 1024))
        _a = jnp.logical_or(_a, jnp.swapaxes(_a, -1, -2))
        _a = jnp.logical_or(_a, jnp.eye(1024, dtype=bool))
        adj = _a.astype(jnp.int32)
        return x, adj
    x, adj = _rec_inputs()
    def _L0_gnn_setup():
        import jax, jax.numpy as jnp
        import numpy as np
        B, N, D, T = (512, 50, 256, 64)
        NEG = -9000000000000000.0
        LRELU_SLOPE = 0.2
        key = jax.random.key(seed)
        k0, k1, k2, k3, k4 = jax.random.split(key, 5)
        hidden = jax.random.normal(k0, (B, N, D), dtype=jnp.float32)
        adj = jax.random.randint(k1, (B, N, N), 0, 6, dtype=jnp.int32)
        A_interval = jax.random.uniform(k2, (B, N, N), dtype=jnp.float32)
        stdv = 1.0 / np.sqrt(D)
        a_rel = jax.random.uniform(k3, (5, D), dtype=jnp.float32, minval=-stdv, maxval=stdv)
        t_rel = jax.random.uniform(k4, (5, T), dtype=jnp.float32, minval=-stdv, maxval=stdv)
        time_w = jnp.asarray(1.0 / 10.0 ** np.linspace(0, 9, T, dtype=np.float32))
        return {'hidden': hidden, 'adj': adj, 'A_interval': A_interval, 'a_rel': a_rel, 't_rel': t_rel, 'time_w': time_w}
    _L0_gnn_all = _L0_gnn_setup()
    _L0_gnn_in = {k: v for k, v in _L0_gnn_all.items() if k in ('a_rel', 't_rel', 'time_w', )}
    del _L0_gnn_all

    return {
        "x": x,
        "adj": adj,
        "L0_gnn_a_rel": _L0_gnn_in["a_rel"],
        "L0_gnn_t_rel": _L0_gnn_in["t_rel"],
        "L0_gnn_time_w": _L0_gnn_in["time_w"],
    }

def reference(x, adj, L0_gnn_a_rel, L0_gnn_t_rel, L0_gnn_time_w):
    import jax
    import jax.numpy as jnp
    def _L0_gnn_ref(hidden, adj, A_interval, a_rel, t_rel, time_w):
        import jax, jax.numpy as jnp
        import numpy as np
        B, N, D, T = (512, 50, 256, 64)
        NEG = -9000000000000000.0
        LRELU_SLOPE = 0.2
        e_struct = jnp.einsum('bid,bjd,rd->bijr', hidden, hidden, a_rel)
        tenc = jax.lax.stop_gradient(jnp.cos(A_interval[..., None] * time_w))
        e_time = jnp.einsum('bijt,rt->bijr', tenc, t_rel)
        e = jax.nn.leaky_relu(e_struct + e_time, negative_slope=LRELU_SLOPE)
        idx = jnp.clip(adj - 1, 0, 4)[..., None]
        sel = jnp.take_along_axis(e, idx, axis=-1)[..., 0]
        alpha = jnp.where((adj >= 1) & (adj <= 5), sel, NEG)
        alpha = jax.nn.softmax(alpha, axis=-1)
        return jnp.einsum('bij,bjd->bid', alpha, hidden)

    x = _layernorm(x + _L0_gnn_ref(x, adj, adj, L0_gnn_a_rel, L0_gnn_t_rel, L0_gnn_time_w), axis=-1)
    return x


_drawn_inputs = setup_inputs


def setup_inputs(seed=0):
    import zlib

    import numpy as np

    out = dict(_drawn_inputs(seed))
    spreads = {}
    factors = {'L0_gnn_t_rel': 4.969, 'L0_gnn_time_w': 8.0}
    for name, (base, spread) in spreads.items():
        noise = np.random.default_rng([zlib.crc32(name.encode()), seed]).standard_normal(out[name].shape)
        drawn = base * np.exp(spread * noise) if base else spread * noise
        out[name] = jnp.asarray(drawn.astype(out[name].dtype))
    for name, factor in factors.items():
        out[name] = (out[name] * factor).astype(out[name].dtype)
    return out
```

```python
import math
from contextlib import ExitStack

import concourse.bass as bass
from concourse import mybir

ALU = mybir.AluOpType
ACT = mybir.ActivationFunctionType
AX_X = mybir.AxisListType.X
F32 = mybir.dt.float32
I32 = mybir.dt.int32

P = 128
NEG = -9.0e15
SLOPE = 0.2
EPS = 1e-5
ROUND = 1.5 * 2.0 ** 23
TWO_PI_HI = 6.28125
TWO_PI_MID = float.fromhex("0x1.fb4p-10")
TWO_PI_LO = 2.0 * math.pi - TWO_PI_HI - TWO_PI_MID
RSQRT_MAGIC = float(0x5F3759DF)
NEWTON_STEPS = 3
NEWTON_OPS = 3 + 3 * NEWTON_STEPS


def relation_attention(nc: bass.Bass, x: bass.AP, adj: bass.AP, a_rel: bass.AP, t_rel: bass.AP, time_w: bass.AP,
                       out: bass.AP):
    B, N, D = x.shape
    R, T = t_rel.shape
    TILES = N // P
    DC = D // P
    BANK = 512
    HALVES = N // BANK
    PER = BANK // P

    with ExitStack() as ctx:
        def sb(name, shape, dt=F32):
            return ctx.enter_context(nc.sbuf_tensor(name, shape, dt))

        def psum(name, shape):
            return ctx.enter_context(nc.psum_tensor(name, shape, F32))

        def sem(name):
            return ctx.enter_context(nc.semaphore(name))

        ident = sb("ident", [P, P])
        ones = sb("ones", [P, P])
        a_cols = sb("a_cols", [P, DC, R])
        w_col = sb("w_col", [T, 1])
        t_cols = sb("t_cols", [T, R])
        phase = sb("phase", [T, 4, R])
        c_all = sb("c_all", [P, R])

        x_b = sb("x_b", [P, TILES, D])
        xT_b = sb("xT_b", [P, DC, N])
        ax_t = sb("ax_t", [P, R, DC, P])
        adj_t = sb("adj_t", [P, N], I32)
        is_rel = sb("is_rel", [P, N], I32)
        biased = sb("biased", [P, N])
        leaky = sb("leaky", [P, N])
        alpha = sb("alpha", [P, N])
        probsT = sb("probsT", [P, TILES, P])
        y_t = sb("y_t", [P, D])
        out_t = sb("out_t", [P, D])
        row = sb("row", [P, 8])
        stats = sb("stats", [P, 6])
        mean_var = sb("mean_var", [P, 2])

        ps_scores = psum("ps_scores", [P, N])
        ps_T = psum("ps_T", [P, TILES, P])
        ps_out = psum("ps_out", [P, BANK])
        ps_c = psum("ps_c", [P, BANK])

        params_loaded = sem("params_loaded")
        ident_zero = sem("ident_zero")
        ident_ready = sem("ident_ready")
        phase_step = sem("phase_step")
        angles_ready = sem("angles_ready")
        cosines_ready = sem("cosines_ready")
        time_terms_ready = sem("time_terms_ready")
        c_summed = sem("c_summed")
        c_ready = sem("c_ready")

        g_x_loaded = sem("g_x_loaded")
        g_adj_loaded = sem("g_adj_loaded")
        g_stored = sem("g_stored")
        g_xT = sem("g_xT")
        g_xT_copied = sem("g_xT_copied")
        g_ax_ready = sem("g_ax_ready")
        g_scores = sem("g_scores")
        g_biased = sem("g_biased")
        g_cleared = sem("g_cleared")
        g_is_rel = sem("g_is_rel")
        g_leaky = sem("g_leaky")
        g_selected = sem("g_selected")
        g_max = sem("g_max")
        g_probs = sem("g_probs")
        g_probsT = sem("g_probsT")
        g_probsT_copied = sem("g_probsT_copied")
        g_pv = sem("g_pv")
        g_inv = sem("g_inv")
        g_y = sem("g_y")
        g_bn = sem("g_bn")
        g_moments = sem("g_moments")
        g_rstd = sem("g_rstd")
        g_normed = sem("g_normed")

        block = ctx.enter_context(nc.Block())

        @block.sync
        def _(sp):
            with nc.allow_non_contiguous_dma(reason="a few hundred words of parameters, once"):
                for k in range(DC):
                    sp.dma_start(a_cols[:, k, :], a_rel[:, k * P:(k + 1) * P].rearrange("r d -> d r")).then_inc(params_loaded, 16)
                sp.dma_start(t_cols[:], t_rel.rearrange("r t -> t r")).then_inc(params_loaded, 16)
                sp.dma_start(w_col[:], time_w.rearrange("(t a) -> t a", a=1)).then_inc(params_loaded, 16)
            with sp.Fori(0, B) as b:
                sp.dma_start(x_b[:], x[bass.ds(b, 1)].rearrange("a (t p) d -> p (a t) d", p=P)).then_inc(g_x_loaded, 16)
                with sp.Fori(0, TILES) as t:
                    sp.dma_start(adj_t[:], adj[bass.ds(b, 1), bass.ds(t * P, P)].rearrange("a p j -> (a p) j")).then_inc(g_adj_loaded, 16)
                    sp.wait_ge(g_normed, b * TILES + t + 1)
                    sp.dma_start(out[bass.ds(b, 1), bass.ds(t * P, P)].rearrange("a p d -> (a p) d"), out_t[:]).then_inc(g_stored, 16)
            sp.wait_ge(g_stored, 16 * B * TILES)

        @block.gpsimd
        def _(pool):
            pool.memset(ident[:], 0.0).then_inc(ident_zero, 1)
            pool.wait_ge(ident_zero, 1)
            pool.affine_select(out=ident[:], in_=ident[:], compare_op=ALU.not_equal, fill=1.0, base=0,
                               pattern=[[-1, P]], channel_multiplier=1).then_inc(ident_ready, 1)

        @block.scalar
        def _(act):
            act.wait_ge(angles_ready, 1)
            act.activation(phase[:, 1, :], phase[:, 0, :], ACT.Sin).then_inc(cosines_ready, 1)
            act.wait_ge(c_ready, 1)
            with act.Fori(0, B) as b:
                for k in range(DC):
                    for h in range(HALVES):
                        act.wait_ge(g_xT, b * (DC * HALVES) + (k * HALVES + h + 1))
                        act.activation(xT_b[:, k, h * BANK:(h + 1) * BANK],
                                       ps_T[:, h * PER:(h + 1) * PER, :].rearrange("p c i -> p (c i)"),
                                       ACT.Copy).then_inc(g_xT_copied, 1)
                with act.Fori(0, TILES) as t:
                    g = b * TILES + t
                    for r in range(R):
                        act.wait_ge(g_scores, g * R + (r + 1))
                        if r > 0:
                            act.wait_ge(g_leaky, g * R + r)
                        act.activation(biased[:], ps_scores[:], ACT.Identity, bias=c_all[:, r:r + 1]).then_inc(g_biased, 1)
                    act.wait_ge(g_max, g + 1)
                    act.activation(alpha[:], alpha[:], ACT.Exp, bias=row[:, 0:1], accum_out=row[:, 1:2]).then_inc(g_probs, 1)
                    act.wait_ge(g_probsT, g + 1)
                    act.activation(probsT[:], ps_T[:], ACT.Copy).then_inc(g_probsT_copied, 1)

        @block.vector
        def _(dve):
            dve.memset(ones[:], 1.0).then_inc(phase_step, 1)
            for r in range(R):
                dve.memset(phase[:, 2, r:r + 1], float(r + 1)).then_inc(phase_step, 1)
            dve.wait_ge(params_loaded, 16 * (DC + 2))
            dve.wait_ge(phase_step, 1 + R)
            n = [1 + R]

            def link(instruction):
                n[0] += 1
                instruction.then_inc(phase_step, 1)
                dve.wait_ge(phase_step, n[0])

            ang, turns = phase[:, 0, :], phase[:, 1, :]
            link(dve.tensor_scalar(ang, phase[:, 2, :], w_col[:, 0:1], None, ALU.mult))
            link(dve.tensor_scalar(turns, ang, 1.0 / (2.0 * math.pi), ROUND, ALU.mult, ALU.add))
            link(dve.tensor_scalar(turns, turns, -ROUND, None, ALU.add))
            for part in (TWO_PI_HI, TWO_PI_MID, TWO_PI_LO):
                link(dve.scalar_tensor_tensor(out=ang, in0=turns, scalar=-part, in1=ang, op0=ALU.mult, op1=ALU.add))
            link(dve.scalar_tensor_tensor(out=ang, in0=ang, scalar=-1.0, in1=ang, op0=ALU.mult, op1=ALU.max))
            dve.tensor_scalar(ang, ang, -1.0, math.pi / 2, ALU.mult, ALU.add).then_inc(angles_ready, 1)
            dve.wait_ge(cosines_ready, 1)
            dve.tensor_tensor(phase[:, 3, :], phase[:, 1, :], t_cols[:], ALU.mult).then_inc(time_terms_ready, 1)
            dve.wait_ge(c_summed, 1)
            dve.tensor_copy(c_all[:], ps_c[:, 0:R]).then_inc(c_ready, 1)

            def newton_rsqrt(step, before, y, v, tmp):
                k = 0

                def then(instruction):
                    nonlocal k
                    k += 1
                    instruction.then_inc(step, 1)
                    dve.wait_ge(step, before + k)

                then(dve.tensor_scalar(v, v, EPS, None, ALU.add))
                then(dve.tensor_scalar(y.bitcast(I32), v.bitcast(I32), 1, None, ALU.logical_shift_right))
                then(dve.tensor_scalar(y.bitcast(I32), y.bitcast(I32), -1.0, RSQRT_MAGIC, ALU.mult, ALU.add))
                for _ in range(NEWTON_STEPS):
                    then(dve.tensor_tensor(tmp, y, y, ALU.mult))
                    then(dve.scalar_tensor_tensor(out=tmp, in0=tmp, scalar=-0.5, in1=v, op0=ALU.mult, op1=ALU.mult))
                    then(dve.scalar_tensor_tensor(out=y, in0=tmp, scalar=1.5, in1=y, op0=ALU.add, op1=ALU.mult))

            with dve.Fori(0, B) as b:
                with dve.Fori(0, TILES) as t:
                    dve.wait_ge(g_xT_copied, b * (DC * HALVES) + DC * HALVES)
                    g = b * TILES + t
                    for r in range(R):
                        for k in range(DC):
                            last = dve.tensor_scalar(ax_t[:, r, k, :], xT_b[:, k, bass.ds(t * P, P)], a_cols[:, k, r:r + 1], None, ALU.mult)
                    last.then_inc(g_ax_ready, 1)
                    dve.memset(alpha[:], NEG).then_inc(g_cleared, 1)
                    dve.wait_ge(g_cleared, g + 1)
                    dve.wait_ge(g_adj_loaded, g * 16 + 16)
                    for r in range(R):
                        if r > 0:
                            dve.wait_ge(g_selected, g * R + r)
                        dve.tensor_scalar(is_rel[:], adj_t[:], float(r + 1), None, ALU.is_equal).then_inc(g_is_rel, 1)
                        dve.wait_ge(g_biased, g * R + (r + 1))
                        dve.scalar_tensor_tensor(out=leaky[:], in0=biased[:], scalar=SLOPE, in1=biased[:],
                                                 op0=ALU.mult, op1=ALU.max).then_inc(g_leaky, 1)
                        dve.wait_ge(c_summed, 1)
                        dve.wait_ge(g_leaky, g * R + (r + 1))
                        dve.wait_ge(g_is_rel, g * R + (r + 1))
                        dve.copy_predicated(alpha[:], is_rel[:], leaky[:]).then_inc(g_selected, 1)
                    dve.wait_ge(g_selected, g * R + R)
                    dve.tensor_reduce(row[:, 4:5], alpha[:], AX_X, ALU.max).then_inc(g_inv, 1)
                    dve.wait_ge(g_inv, g * 2 + 1)
                    dve.tensor_scalar(row[:, 0:1], row[:, 4:5], -1.0, None, ALU.mult).then_inc(g_max, 1)
                    dve.wait_ge(g_probs, g + 1)
                    dve.reciprocal(row[:, 2:3], row[:, 1:2]).then_inc(g_inv, 1)
                    dve.wait_ge(g_inv, g * 2 + 2)
                    dve.wait_ge(g_pv, g + 1)
                    dve.scalar_tensor_tensor(out=y_t[:], in0=ps_out[:, 0:D], scalar=row[:, 2:3], in1=x_b[:, bass.ds(t, 1), :].rearrange("p a d -> p (a d)"),
                                             op0=ALU.mult, op1=ALU.add).then_inc(g_y, 1)
                    dve.wait_ge(g_y, g + 1)
                    dve.bn_stats(stats[:], y_t[:]).then_inc(g_bn, 1)
                    dve.wait_ge(c_summed, 1)
                    dve.wait_ge(g_bn, g + 1)
                    dve.bn_aggr(mean_var[:], stats[:]).then_inc(g_moments, 1)
                    dve.wait_ge(g_moments, g + 1)
                    newton_rsqrt(g_rstd, g * NEWTON_OPS, row[:, 3:4], mean_var[:, 1:2], row[:, 5:6])
                    dve.tensor_scalar(out_t[:], y_t[:], mean_var[:, 0:1], row[:, 3:4], ALU.subtract, ALU.mult).then_inc(g_normed, 1)
                    dve.wait_ge(g_stored, g * 16 + 16)

        @block.tensor
        def _(pe):
            pe.wait_ge(phase_step, 1)
            pe.wait_ge(time_terms_ready, 1)
            pe.matmul(ps_c[:, 0:R], ones[0:T, :], phase[:, 3, :], start=True, stop=True).then_inc(c_summed, 1)
            pe.wait_ge(ident_ready, 1)
            with pe.Fori(0, B) as b:
                pe.wait_ge(g_x_loaded, b * 16 + 16)
                for k in range(DC):
                    for h in range(HALVES):
                        if k + h > 0:
                            pe.wait_ge(g_xT_copied, b * (DC * HALVES) + (k * HALVES + h))
                        for c in range(h * PER, (h + 1) * PER):
                            last = pe.transpose(ps_T[:, c, :], x_b[:, c, k * P:(k + 1) * P], ident[:])
                        last.then_inc(g_xT, 1)
                with pe.Fori(0, TILES) as t:
                    g = b * TILES + t
                    pe.wait_ge(g_ax_ready, g + 1)
                    for r in range(R):
                        if r > 0:
                            pe.wait_ge(g_biased, g * R + r)
                        for h in range(HALVES):
                            for k in range(DC):
                                last = pe.matmul(ps_scores[:, h * BANK:(h + 1) * BANK], ax_t[:, r, k, :],
                                                 xT_b[:, k, h * BANK:(h + 1) * BANK], start=(k == 0), stop=(k == DC - 1))
                        last.then_inc(g_scores, 1)
                    pe.wait_ge(g_probs, g + 1)
                    for c in range(TILES):
                        last = pe.transpose(ps_T[:, c, :], alpha[:, c * P:(c + 1) * P], ident[:])
                    last.then_inc(g_probsT, 1)
                    pe.wait_ge(g_probsT_copied, g + 1)
                    for c in range(TILES):
                        last = pe.matmul(ps_out[:, 0:D], probsT[:, c, :], x_b[:, c, :], start=(c == 0), stop=(c == TILES - 1))
                    last.then_inc(g_pv, 1)


_INS = ["x", "adj", "L0_gnn_a_rel", "L0_gnn_t_rel", "L0_gnn_time_w"]


def kernel(**inputs):
    import numpy as _np
    import concourse.bacc as _bacc
    from concourse import mybir as _mybir
    from concourse.bass_utils import run_bass_kernel_spmd as _run

    nc = _bacc.Bacc("TRN2", target_bir_lowering=False, num_devices=1)
    arrays, args = {}, []
    for name in _INS:
        a = _np.ascontiguousarray(inputs[name])
        arrays[f"in_{name}_dram"] = a
        args.append(nc.dram_tensor(f"in_{name}_dram", a.shape, _mybir.dt.from_np(a.dtype), kind="ExternalInput").ap())
    shape = tuple(inputs["x"].shape)
    args.append(nc.dram_tensor("out_0_dram", shape, _mybir.dt.float32, kind="ExternalOutput").ap())
    relation_attention(nc, *args)
    r = _run(nc, [arrays], core_ids=[0])
    return r.results[0]["out_0_dram"]
```

```python
import math
from contextlib import ExitStack

import concourse.bass as bass
from concourse import mybir

ALU = mybir.AluOpType
ACT = mybir.ActivationFunctionType
AX_X = mybir.AxisListType.X
F32 = mybir.dt.float32
F32R = mybir.dt.float32r
BF16 = mybir.dt.bfloat16
I32 = mybir.dt.int32

P = 128
BANK = 512
NEG = -9.0e15
SLOPE = 0.2
EPS = 1e-5
MASKED = 2.0 ** 80
SUSPECT = 2.0 ** 78
ROUND = 1.5 * 2.0 ** 23
TWO_PI_HI = 6.28125
TWO_PI_MID = float.fromhex("0x1.fb4p-10")
TWO_PI_LO = 2.0 * math.pi - TWO_PI_HI - TWO_PI_MID
RSQRT_MAGIC = float(0x5F3759DF)
NEWTON_STEPS = 3
NEWTON_OPS = 3 + 3 * NEWTON_STEPS
PLACES = 7

SETS = [
    [[(1, 0, 2), (0, 0, 1)]],
    [[(2, 0, 3)]],
    [[(3, 0, 4)]],
    [[(4, 0, 3)]],
    [[(4, 3, 2)], [(5, 0, 3)]],
    [[(5, 3, 3)], [(6, 0, 4)]],
    [[(6, 4, 3)], [(7, 0, 4)]],
    [[(7, 4, 4)]],
]
GROUPS = sum(len(s) for s in SETS)
GROUPS_BEFORE = [sum(len(s) for s in SETS[:k]) for k in range(len(SETS))]
GROUPS_TO_ROW = [max(n + 1 for n, g in enumerate(sum(SETS, [])) if any(r == row for r, _, _ in g)) for row in range(8)]

ADJ_SLOTS = 4
APPLIED = [(), (), (), (), (0, 1, 2), (3, 4, 5), (6, 7), ()]
LAST_PARTS = [(0, 6), (6, 8)]
POOL_APPLIES = [(4, 5), (6,)]
ACT_APPLIES = [(0, 1, 2, 3), (7,)]
PREP = 12
SCORES = 10
PAIR = 16


def triangle(row):
    return (2, 0)[row] if row < 2 else row * (row + 1) // 2


def relation_attention(nc: bass.Bass, x: bass.AP, adj: bass.AP, a_rel: bass.AP, t_rel: bass.AP, time_w: bass.AP,
                       out: bass.AP):
    B, N, D = x.shape
    R, T = t_rel.shape
    TILES = N // P
    ALL = B * TILES
    DC = D // P
    HALVES = N // BANK
    PER = BANK // P
    BLOCKS = triangle(TILES)
    STORES = (B // 2, B // 2 - 1 + len(LAST_PARTS))
    assert TILES == len(SETS) and PAIR == 2 * TILES and ALL % PAIR == 0

    with ExitStack() as ctx:
        def sb(name, shape, dt=F32):
            return ctx.enter_context(nc.sbuf_tensor(name, shape, dt))

        def psum(name, shape):
            return ctx.enter_context(nc.psum_tensor(name, shape, F32))

        def sem(name):
            return ctx.enter_context(nc.semaphore(name))

        ident = sb("ident", [P, P])
        ones = sb("ones", [P, P])
        a_cols = sb("a_cols", [P, DC, R])
        neg_a = sb("neg_a", [P, DC, P])
        w_col = sb("w_col", [T, 1])
        t_cols = sb("t_cols", [T, R])
        phase = sb("phase", [T, 4, R])
        c_all = sb("c_all", [P, R])
        neg_c = sb("neg_c", [P, 2])

        x_rows = sb("x_rows", [P, PAIR, D])
        x_hi = sb("x_hi", [P, 2, TILES, D], F32R)
        x_lo = sb("x_lo", [P, 2, TILES, D], F32R)
        xT_hi = sb("xT_hi", [P, 2, DC, N], F32R)
        xT_lo = sb("xT_lo", [P, 2, DC, N], F32R)
        ax = sb("ax", [P, 2, DC, P])
        ax_hi = sb("ax_hi", [P, TILES, DC, P], F32R)
        ax_lo = sb("ax_lo", [P, TILES, DC, P], F32R)
        slope = sb("slope", [P, 2, BANK])
        scores = sb("scores", [P, 2, BLOCKS, P])
        adj_rows = sb("adj_rows", [P, ADJ_SLOTS, N], I32)
        mask = sb("mask", [P, 2, N], BF16)
        probs = sb("probs", [P, 2, N])
        pT_hi = sb("pT_hi", [P, 2, TILES, P], F32R)
        pT_lo = sb("pT_lo", [P, 2, TILES, P], F32R)
        y = sb("y", [P, 2, TILES, D])
        lows = sb("lows", [P, PAIR, 2])
        low = sb("low", [P, PAIR])
        sums = sb("sums", [P, PAIR])
        inv = sb("inv", [P, PAIR])
        stats = sb("stats", [P, PAIR, 6])
        moments = sb("moments", [P, 2, TILES, 2])
        rstd = sb("rstd", [P, 2, TILES])
        shift = sb("shift", [P, 2, TILES])
        newton = sb("newton", [P, TILES])
        extremes = sb("extremes", [P, 2, TILES])
        suspect = sb("suspect", [P, 4])
        flag = sb("flag", [1, 1], I32)

        ps_scores = psum("ps_scores", [P, 2, BANK])
        ps_sT = psum("ps_sT", [P, N])
        ps_pT = psum("ps_pT", [P, TILES, P])
        ps_o = psum("ps_o", [P, D])
        ps_x = psum("ps_x", [P, DC, P])

        g_x = x_rows[:, 0:TILES, :]
        g_xT = scores[:, 0, 0:2 * TILES, :].rearrange("p (k c) i -> p k (c i)", k=DC)
        g_ax = scores[:, 0, 2 * TILES:2 * TILES + R * DC, :].rearrange("p (r k) i -> p r k i", r=R)
        g_biased = scores[:, 1, 0:TILES, :].rearrange("p c i -> p (c i)")
        g_leaky = scores[:, 1, TILES:2 * TILES, :].rearrange("p c i -> p (c i)")
        g_pT = scores[:, 1, 2 * TILES:3 * TILES, :]
        g_alpha = probs[:, 0, :]
        g_adj = adj_rows[:, 0, :]
        g_is_rel = adj_rows[:, 1, :]
        g_y = y[:, 0, 0, :]
        g_out = y[:, 0, 1, :]

        factors_loaded = sem("factors_loaded")
        params_loaded = sem("params_loaded")
        ident_zero = sem("ident_zero")
        ident_ready = sem("ident_ready")
        setup_step = sem("setup_step")
        angles_ready = sem("angles_ready")
        cosines_ready = sem("cosines_ready")
        time_terms_ready = sem("time_terms_ready")
        c_summed = sem("c_summed")
        c_ready = sem("c_ready")

        x_loaded = [sem(f"x_loaded_{k}") for k in range(PAIR // 2)]
        adj_loaded = [sem(f"adj_loaded_{k}") for k in range(ADJ_SLOTS)]
        out_stored = [sem(f"out_stored_{k}") for k in range(2)]
        mask_ready = sem("mask_ready")
        x_hi_ready = sem("x_hi_ready")
        x_lo_ready = sem("x_lo_ready")
        xT_ready = sem("xT_ready")
        xT_hi_ready = sem("xT_hi_ready")
        xT_lo_ready = sem("xT_lo_ready")
        ax_ready = sem("ax_ready")
        ax_hi_ready = sem("ax_hi_ready")
        ax_lo_ready = sem("ax_lo_ready")
        group_multiplied = sem("group_multiplied")
        slope_ready = sem("slope_ready")
        group_stored = sem("group_stored")
        sT_ready = sem("sT_ready")
        masked_part = sem("masked_part")
        low_ready = sem("low_ready")
        probs_ready = sem("probs_ready")
        pT_ready = sem("pT_ready")
        pT_hi_ready = sem("pT_hi_ready")
        pT_lo_ready = sem("pT_lo_ready")
        o_ready = sem("o_ready")
        o_scaled = sem("o_scaled")
        inv_ready = sem("inv_ready")
        y_ready = sem("y_ready")
        stats_ready = sem("stats_ready")
        moments_ready = sem("moments_ready")
        extremes_step = sem("extremes_step")
        norm_step = sem("norm_step")
        norm_ready = sem("norm_ready")
        applied = sem("applied")
        applied_by_act = sem("applied_by_act")
        suspect_step = sem("suspect_step")
        suspect_ready = sem("suspect_ready")
        suspects_summed = sem("suspects_summed")
        flag_ready = sem("flag_ready")

        g_x_loaded = sem("g_x_loaded")
        g_adj_loaded = sem("g_adj_loaded")
        g_stored = sem("g_stored")
        g_xT_ready = sem("g_xT_ready")
        g_xT_copied = sem("g_xT_copied")
        g_ax_ready = sem("g_ax_ready")
        g_scores_ready = sem("g_scores_ready")
        g_biased_ready = sem("g_biased_ready")
        g_cleared = sem("g_cleared")
        g_is_rel_ready = sem("g_is_rel_ready")
        g_leaky_ready = sem("g_leaky_ready")
        g_selected = sem("g_selected")
        g_peak = sem("g_peak")
        g_low_ready = sem("g_low_ready")
        g_probs_ready = sem("g_probs_ready")
        g_pT_ready = sem("g_pT_ready")
        g_pT_copied = sem("g_pT_copied")
        g_o_ready = sem("g_o_ready")
        g_inv_ready = sem("g_inv_ready")
        g_y_ready = sem("g_y_ready")
        g_stats_ready = sem("g_stats_ready")
        g_moments_ready = sem("g_moments_ready")
        g_rstd_step = sem("g_rstd_step")
        g_normed = sem("g_normed")

        x_blocks = x.rearrange("b (t p) d -> p (b t) d", p=P)
        out_blocks = out.rearrange("b (t p) d -> p (b t) d", p=P)
        adj_tiles = adj.rearrange("b (t p) j -> p (b t) j", p=P)

        def until(engine, semaphore, count, loop, per_pair):
            if loop is not None:
                engine.wait_ge(semaphore, loop * per_pair + count)
            elif count > 0:
                engine.wait_ge(semaphore, count)

        def until_all(engine, loop, *needs):
            if loop is None:
                for semaphore, count, per_pair in needs:
                    until(engine, semaphore, count, loop, per_pair)
                return
            values = [engine.to_reg(loop * per_pair + count) for _, count, per_pair in needs]
            engine.wait_ge(ident_ready, 1)
            for (semaphore, _, _), value in zip(needs, values):
                engine.wait_ge(semaphore, value)

        def steps(engine, step, first, last):
            for q in range(first, PAIR):
                step(q, None)
            with engine.Fori(1, ALL // PAIR - 1) as pair:
                for q in range(PAIR):
                    step(q, pair)
            for q in range(ALL - PAIR, last):
                step(q, None)

        def present(index, loop):
            return loop is not None or 0 <= index < ALL

        def blocks_at(q, loop):
            if loop is not None or q >= 0:
                return [q + PREP] if present(q + PREP, loop) else []
            return [0, 1] if q == -PREP else [q + PREP + 1] if q < -1 else []

        def x_place(g, loop):
            if loop is None and g < PREP and g % 2 == 1:
                return ps_o[:].rearrange("p (k i) -> p k i", k=DC)
            return ps_x[:]

        block = ctx.enter_context(nc.Block())

        @block.sync
        def _(sp):
            def at(index, loop, size):
                return bass.ds(loop * PAIR + index, size) if loop is not None else slice(index, index + size)

            def step(q, loop):
                g = q + PREP + 2
                if g % 2 == 0 and present(g, loop):
                    until(sp, y_ready, g + 2 - PAIR, loop, PAIR)
                    sp.dma_start(x_rows[:, g % PAIR:g % PAIR + 2, :], x_blocks[:, at(g, loop, 2), :]).then_inc(x_loaded[g % PAIR // 2], 16)
                j = q + 5
                if present(j, loop):
                    until(sp, mask_ready, j - ADJ_SLOTS + 1, loop, PAIR)
                    sp.dma_start(adj_rows[:, j % ADJ_SLOTS, :], adj_tiles[:, at(j, loop, 1), :].rearrange("p a j -> p (a j)")).then_inc(adj_loaded[j % ADJ_SLOTS], 16)
                if q % TILES == TILES - 1 and present(q + 1 - 2 * TILES, loop):
                    done = q + 1 - 2 * TILES
                    until(sp, applied, done + TILES, loop, PAIR)
                    sp.dma_start(out_blocks[:, at(done, loop, TILES), :], y[:, done // TILES % 2, :, :]).then_inc(out_stored[done // TILES % 2], 16)

            def general():
                with sp.Fori(0, B) as b:
                    sp.dma_start(g_x, x_blocks[:, bass.ds(b * TILES, TILES), :]).then_inc(g_x_loaded, 16)
                    with sp.Fori(0, TILES) as t:
                        sp.dma_start(g_adj, adj_tiles[:, bass.ds(b * TILES + t, 1), :].rearrange("p a j -> p (a j)")).then_inc(g_adj_loaded, 16)
                        sp.wait_ge(g_normed, b * TILES + t + 1)
                        sp.dma_start(out_blocks[:, bass.ds(b * TILES + t, 1), :].rearrange("p a d -> p (a d)"), g_out).then_inc(g_stored, 16)
                sp.wait_ge(g_stored, 16 * ALL)

            for q in range(-PREP - 2, -PREP):
                step(q, None)
            steps(sp, step, -PREP, ALL)
            for k, (first, last) in enumerate(LAST_PARTS):
                sp.wait_ge(applied, ALL - TILES + sum(len(tiles) for tiles in POOL_APPLIES[:k + 1]))
                sp.wait_ge(applied_by_act, sum(len(tiles) for tiles in ACT_APPLIES[:k + 1]))
                sp.dma_start(out_blocks[:, ALL - TILES + first:ALL - TILES + last, :], y[:, 1, first:last, :]).then_inc(out_stored[1], 16)
            for stored, stores in zip(out_stored, STORES):
                sp.wait_ge(stored, 16 * stores)
            sp.wait_ge(flag_ready, 1)
            with sp.If(sp.value_load(flag[0:1, 0:1]) != 0):
                general()

        @block.gpsimd
        def _(pool):
            pool.memset(ident[:], 0.0).then_inc(ident_zero, 1)
            pool.wait_ge(ident_zero, 1)
            pool.affine_select(out=ident[:], in_=ident[:], compare_op=ALU.not_equal, fill=1.0, base=0,
                               pattern=[[-1, P]], channel_multiplier=1).then_inc(ident_ready, 1)

            def make_mask(j, loop):
                until_all(pool, loop, (adj_loaded[j % ADJ_SLOTS], 16 * (j // ADJ_SLOTS + 1), 16 * PAIR // ADJ_SLOTS), (low_ready, j - 1, PAIR))
                pool.tensor_scalar(mask[:, j % 2, :], adj_rows[:, j % ADJ_SLOTS, :], -1.0, -MASKED, ALU.add, ALU.mult).then_inc(mask_ready, 1)

            def split_x(g, loop):
                half, c = g // TILES % 2, g % TILES
                until_all(pool, loop, (x_loaded[g % PAIR // 2], 16 * (g // PAIR + 1), 16),
                          (o_ready, (g // TILES - 1) * TILES, PAIR))
                pool.tensor_scalar(x_hi[:, half, c, :], x_rows[:, g % PAIR, :], 1.0, 1.0, ALU.mult, ALU.mult).then_inc(x_hi_ready, 1)
                until(pool, x_hi_ready, g + 1, loop, PAIR)
                pool.tensor_tensor(x_lo[:, half, c, :], x_rows[:, g % PAIR, :], x_hi[:, half, c, :].bitcast(F32),
                                   ALU.subtract).then_inc(x_lo_ready, 1)

            def split_ax(g, loop):
                until(pool, ax_hi_ready, g + 1, loop, PAIR)
                pool.tensor_tensor(ax_lo[:, g % TILES, :, :], ax[:, g % 2, :, :], ax_hi[:, g % TILES, :, :].bitcast(F32),
                                   ALU.subtract).then_inc(ax_lo_ready, 1)

            def add_x(q, loop):
                until(pool, o_scaled, q + 1, loop, PAIR)
                pool.tensor_tensor(y[:, q // TILES % 2, q % TILES, :], y[:, q // TILES % 2, q % TILES, :], x_rows[:, q % PAIR, :],
                                   ALU.add).then_inc(y_ready, 1)

            def apply_norm(g, loop, part=0):
                half, c = g // TILES % 2, g % TILES
                until_all(pool, loop, (norm_ready, g // TILES + 1 + part, 2))
                pool.tensor_scalar(y[:, half, c, :], y[:, half, c, :], rstd[:, half, c:c + 1], shift[:, half, c:c + 1],
                                   ALU.mult, ALU.add).then_inc(applied, 1)

            def step(q, loop):
                if present(q + 2, loop):
                    make_mask(q + 2, loop)
                if present(q + PREP, loop):
                    split_ax(q + PREP, loop)
                if present(q + TILES, loop):
                    split_x(q + TILES, loop)
                if present(q - 1, loop):
                    add_x(q - 1, loop)
                for c in APPLIED[q % TILES]:
                    g = q - q % TILES - TILES + c
                    if present(g, loop):
                        apply_norm(g, loop)

            steps(pool, step, -PREP, ALL)
            for c in POOL_APPLIES[0]:
                apply_norm(ALL - TILES + c, None)
            step(ALL, None)
            for c in POOL_APPLIES[1]:
                apply_norm(ALL - TILES + c, None, part=1)

        @block.scalar
        def _(act):
            with nc.allow_non_contiguous_dma(reason="a few hundred words of parameters, once"):
                for k in range(DC):
                    act.dma_start(a_cols[:, k, :], a_rel[:, k * P:(k + 1) * P].rearrange("r d -> d r")).then_inc(factors_loaded, 16)
                act.dma_start(w_col[:], time_w.rearrange("(t a) -> t a", a=1)).then_inc(params_loaded, 16)
                act.dma_start(t_cols[:], t_rel.rearrange("r t -> t r")).then_inc(params_loaded, 16)

            def copy_pT(q, loop):
                for h in range(HALVES):
                    until(act, pT_ready, 2 * q + h + 1, loop, 2 * PAIR)
                    if h == 0:
                        until(act, o_ready, q - 1, loop, PAIR)
                    act.activation(pT_hi[:, q % 2, h * PER:(h + 1) * PER, :], ps_pT[:, h * PER:(h + 1) * PER, :],
                                   ACT.Copy).then_inc(pT_hi_ready, 1)

            def slopes(s, loop):
                for k, group in enumerate(SETS[s % TILES]):
                    n = s // TILES * GROUPS + GROUPS_BEFORE[s % TILES] + k
                    width = P * sum(count for _, _, count in group)
                    until(act, group_multiplied, n + 1, loop, 2 * GROUPS)
                    until(act, group_stored, n - 1, loop, 2 * GROUPS)
                    act.activation(slope[:, n % 2, 0:width], ps_scores[:, n % 2, 0:width], ACT.Identity,
                                   bias=neg_c[:, 1:2], scale=SLOPE).then_inc(slope_ready, 1)

            def copy_xT(g, loop):
                until(act, xT_ready, g + 1, loop, PAIR)
                until(act, group_multiplied, (g // TILES - 1) * GROUPS, loop, 2 * GROUPS)
                c = g % TILES * P
                act.activation(xT_hi[:, g // TILES % 2, :, c:c + P], x_place(g, loop), ACT.Copy).then_inc(xT_hi_ready, 1)

            def exponentials(q, loop):
                until(act, low_ready, q + 1, loop, PAIR)
                act.activation(probs[:, q % 2, :], probs[:, q % 2, :], ACT.Exp, bias=low[:, q % PAIR:q % PAIR + 1],
                               scale=-1.0, accum_out=sums[:, q % PAIR:q % PAIR + 1]).then_inc(probs_ready, 1)

            def copy_ax(g, loop):
                until(act, ax_ready, g + 1, loop, PAIR)
                until(act, group_multiplied, (g // TILES - 1) * GROUPS + GROUPS_TO_ROW[g % TILES], loop, 2 * GROUPS)
                act.activation(ax_hi[:, g % TILES, :, :], ax[:, g % 2, :, :], ACT.Copy).then_inc(ax_hi_ready, 1)

            def scale_o(q, loop):
                until(act, inv_ready, q + 1, loop, PAIR)
                until(act, o_ready, q + 1, loop, PAIR)
                if q % TILES == 0:
                    until(act, out_stored[q // TILES % 2], 16 * (q // PAIR), loop, 16)
                act.activation(y[:, q // TILES % 2, q % TILES, :], ps_o[:], ACT.Copy,
                               scale=inv[:, q % PAIR:q % PAIR + 1]).then_inc(o_scaled, 1)

            def apply_last(part):
                act.wait_ge(norm_ready, B + part)
                for c in ACT_APPLIES[part]:
                    act.activation(y[:, 1, c, :], y[:, 1, c, :], ACT.Identity, bias=shift[:, 1, c:c + 1],
                                   scale=rstd[:, 1, c:c + 1]).then_inc(applied_by_act, 1)

            def step(q, loop):
                if present(q, loop):
                    copy_pT(q, loop)
                for g in blocks_at(q, loop):
                    copy_xT(g, loop)
                if present(q + 1, loop):
                    exponentials(q + 1, loop)
                if present(q + PREP, loop):
                    copy_ax(q + PREP, loop)
                if present(q - 1, loop):
                    scale_o(q - 1, loop)
                if q == -SCORES - 1:
                    act.wait_ge(angles_ready, 1)
                    act.activation(phase[:, 1, :], phase[:, 0, :], ACT.Sin).then_inc(cosines_ready, 1)
                if q == -SCORES:
                    act.wait_ge(c_ready, 3)
                if present(q + SCORES, loop):
                    slopes(q + SCORES, loop)

            def general():
                with act.Fori(0, B) as b:
                    for k in range(DC):
                        for h in range(HALVES):
                            act.wait_ge(g_xT_ready, b * (DC * HALVES) + (k * HALVES + h + 1))
                            act.activation(g_xT[:, k, h * BANK:(h + 1) * BANK],
                                           ps_pT[:, h * PER:(h + 1) * PER, :].rearrange("p c i -> p (c i)"),
                                           ACT.Copy).then_inc(g_xT_copied, 1)
                    with act.Fori(0, TILES) as t:
                        g = b * TILES + t
                        for r in range(R):
                            act.wait_ge(g_scores_ready, g * R + (r + 1))
                            if r > 0:
                                act.wait_ge(g_leaky_ready, g * R + r)
                            act.activation(g_biased, ps_sT[:], ACT.Identity, bias=c_all[:, r:r + 1]).then_inc(g_biased_ready, 1)
                        act.wait_ge(g_low_ready, g + 1)
                        act.activation(g_alpha, g_alpha, ACT.Exp, bias=low[:, 0:1], accum_out=sums[:, 0:1]).then_inc(g_probs_ready, 1)
                        act.wait_ge(g_pT_ready, g + 1)
                        act.activation(g_pT, ps_pT[:], ACT.Copy).then_inc(g_pT_copied, 1)

            steps(act, step, -PREP, ALL)
            apply_last(0)
            step(ALL, None)
            apply_last(1)
            act.wait_ge(flag_ready, 1)
            with act.If(act.value_load(flag[0:1, 0:1]) != 0):
                general()

        @block.vector
        def _(dve):
            def newton_rsqrt(k, result, value, tmp):
                if k == 0:
                    return dve.tensor_scalar(value, value, EPS, None, ALU.add)
                if k == 1:
                    return dve.tensor_scalar(result.bitcast(I32), value.bitcast(I32), 1, None, ALU.logical_shift_right)
                if k == 2:
                    return dve.tensor_scalar(result.bitcast(I32), result.bitcast(I32), -1.0, RSQRT_MAGIC, ALU.mult, ALU.add)
                if k % 3 == 0:
                    return dve.tensor_tensor(tmp, result, result, ALU.mult)
                if k % 3 == 1:
                    return dve.scalar_tensor_tensor(out=tmp, in0=tmp, scalar=-0.5, in1=value, op0=ALU.mult, op1=ALU.mult)
                return dve.scalar_tensor_tensor(out=result, in0=tmp, scalar=1.5, in1=result, op0=ALU.add, op1=ALU.mult)

            def parameters():
                dve.memset(ones[:], 1.0).then_inc(setup_step, 1)
                dve.memset(extremes[:], 0.0).then_inc(setup_step, 1)
                for r in range(R):
                    dve.memset(phase[:, 2, r:r + 1], float(r + 1)).then_inc(setup_step, 1)
                dve.wait_ge(setup_step, R + 2)
                dve.wait_ge(factors_loaded, 16 * DC)
                for k in range(DC):
                    dve.tensor_scalar(neg_a[:, k, :], ones[:], a_cols[:, k, 0:1], -1.0, ALU.mult, ALU.mult).then_inc(setup_step, 1)
                dve.wait_ge(setup_step, R + 2 + DC)

            def angles():
                count = R + 2 + DC
                dve.wait_ge(params_loaded, 16 * 2)

                def after(instruction):
                    nonlocal count
                    count += 1
                    instruction.then_inc(setup_step, 1)
                    dve.wait_ge(setup_step, count)

                angle, turns = phase[:, 0, :], phase[:, 1, :]
                after(dve.tensor_scalar(angle, phase[:, 2, :], w_col[:, 0:1], None, ALU.mult))
                after(dve.tensor_scalar(turns, angle, 1.0 / (2.0 * math.pi), ROUND, ALU.mult, ALU.add))
                after(dve.tensor_scalar(turns, turns, -ROUND, None, ALU.add))
                for part in (TWO_PI_HI, TWO_PI_MID, TWO_PI_LO):
                    after(dve.scalar_tensor_tensor(out=angle, in0=turns, scalar=-part, in1=angle, op0=ALU.mult, op1=ALU.add))
                after(dve.scalar_tensor_tensor(out=angle, in0=angle, scalar=-1.0, in1=angle, op0=ALU.mult, op1=ALU.max))
                dve.tensor_scalar(angle, angle, -1.0, math.pi / 2, ALU.mult, ALU.add).then_inc(angles_ready, 1)

            def time_terms():
                dve.wait_ge(cosines_ready, 1)
                dve.tensor_tensor(phase[:, 3, :], phase[:, 1, :], t_cols[:], ALU.mult).then_inc(time_terms_ready, 1)
                dve.wait_ge(c_summed, 1)
                dve.tensor_copy(c_all[:], ps_pT[:, 0, 0:R]).then_inc(c_ready, 1)
                dve.wait_ge(c_ready, 1)
                dve.tensor_scalar(neg_c[:, 0:1], c_all[:, 0:1], -1.0, None, ALU.mult).then_inc(c_ready, 1)
                dve.tensor_scalar(neg_c[:, 1:2], c_all[:, 0:1], -SLOPE, None, ALU.mult).then_inc(c_ready, 1)
                dve.wait_ge(c_ready, 3)

            def lower_pT(q, h, loop):
                c = slice(h * PER, (h + 1) * PER)
                until(dve, pT_hi_ready, 2 * q + h + 1, loop, 2 * PAIR)
                dve.tensor_tensor(pT_lo[:, q % 2, c, :], ps_pT[:, c, :], pT_hi[:, q % 2, c, :].bitcast(F32),
                                  ALU.subtract).then_inc(pT_lo_ready, 1)

            def mask_scores(q, loop):
                t, slot = q % TILES, q % PAIR
                split = (t + 1) * P
                until_all(dve, loop, (mask_ready, q + 1, PAIR), (group_stored, (q // TILES + 1) * GROUPS, 2 * GROUPS),
                          (pT_ready, 2 * q - 2, 2 * PAIR))
                own = scores[:, q // TILES % 2, triangle(t):triangle(t) + t + 1, :].rearrange("p c i -> p (c i)")
                first = dve.tensor_tensor_reduce(out=probs[:, q % 2, 0:split], in0=own, in1=mask[:, q % 2, 0:split],
                                                 scale=1.0, scalar=3.0e38, op0=ALU.add, op1=ALU.min,
                                                 accum_out=lows[:, slot, 0:1] if t < TILES - 1 else low[:, slot:slot + 1])
                if t == TILES - 1:
                    first.then_inc(low_ready, 1)
                    return
                until_all(dve, loop, (sT_ready, q // TILES * (TILES - 1) + t + 1, 2 * (TILES - 1)))
                dve.tensor_tensor_reduce(out=probs[:, q % 2, split:N], in0=ps_sT[:, split:N], in1=mask[:, q % 2, split:N],
                                         scale=1.0, scalar=3.0e38, op0=ALU.add, op1=ALU.min,
                                         accum_out=lows[:, slot, 1:2]).then_inc(masked_part, 1)

            def join_lows(q, loop):
                t, slot = q % TILES, q % PAIR
                if t == TILES - 1:
                    return
                until(dve, masked_part, q // TILES * (TILES - 1) + t + 1, loop, 2 * (TILES - 1))
                dve.tensor_tensor(low[:, slot:slot + 1], lows[:, slot, 0:1], lows[:, slot, 1:2], ALU.min).then_inc(low_ready, 1)

            def store_scores(s, loop):
                for k, group in enumerate(SETS[s % TILES]):
                    n = s // TILES * GROUPS + GROUPS_BEFORE[s % TILES] + k
                    row, column, _ = group[0]
                    count = sum(count for _, _, count in group)
                    place = triangle(row) + column
                    until(dve, slope_ready, n + 1, loop, 2 * GROUPS)
                    dve.scalar_tensor_tensor(out=scores[:, s // TILES % 2, place:place + count, :].rearrange("p c i -> p (c i)"),
                                             in0=ps_scores[:, n % 2, 0:count * P], scalar=neg_c[:, 0:1],
                                             in1=slope[:, n % 2, 0:count * P], op0=ALU.add, op1=ALU.min).then_inc(group_stored, 1)

            def scale_x(g, loop):
                c = g % TILES * P
                until(dve, xT_hi_ready, g + 1, loop, PAIR)
                until(dve, ax_lo_ready, g - 1, loop, PAIR)
                dve.tensor_tensor(ax[:, g % 2, :, :], x_place(g, loop), neg_a[:], ALU.mult).then_inc(ax_ready, 1)
                dve.tensor_tensor(xT_lo[:, g // TILES % 2, :, c:c + P], x_place(g, loop),
                                  xT_hi[:, g // TILES % 2, :, c:c + P].bitcast(F32), ALU.subtract).then_inc(xT_lo_ready, 1)

            def invert(q, loop):
                until(dve, probs_ready, q + 1, loop, PAIR)
                dve.reciprocal(inv[:, q % PAIR:q % PAIR + 1], sums[:, q % PAIR:q % PAIR + 1]).then_inc(inv_ready, 1)

            def row_stats(q, loop):
                until(dve, y_ready, q + 1, loop, PAIR)
                dve.bn_stats(stats[:, q % PAIR, :], y[:, q // TILES % 2, q % TILES, :]).then_inc(stats_ready, 1)

            def row_moments(q, loop):
                until_all(dve, loop, (stats_ready, q + 1, PAIR))
                dve.bn_aggr(moments[:, q // TILES % 2, q % TILES, :], stats[:, q % PAIR, :]).then_inc(moments_ready, 1)

            def normaliser(q, place, loop):
                k = (q % TILES - 2) * PLACES + place
                n = q // TILES - 1
                if not 0 <= k <= NEWTON_OPS or not present(n * TILES, loop) or n == B - 1:
                    return
                half = n % 2
                mean, var = moments[:, half, :, 0], moments[:, half, :, 1]
                if k == 0:
                    until(dve, moments_ready, (n + 1) * TILES, loop, PAIR)
                else:
                    until(dve, norm_step, n * NEWTON_OPS + k, loop, 2 * NEWTON_OPS)
                if k < NEWTON_OPS:
                    newton_rsqrt(k, rstd[:, half, :], var, newton[:]).then_inc(norm_step, 1)
                else:
                    dve.scalar_tensor_tensor(out=shift[:, half, :], in0=mean, scalar=-1.0, in1=rstd[:, half, :],
                                             op0=ALU.mult, op1=ALU.mult).then_inc(norm_ready, 1)

            def normaliser_of_last(part):
                first, last = LAST_PARTS[part]
                mean, var = moments[:, 1, first:last, 0], moments[:, 1, first:last, 1]
                result = rstd[:, 1, first:last]
                dve.wait_ge(moments_ready, ALL - TILES + last)
                for k in range(NEWTON_OPS):
                    newton_rsqrt(k, result, var, newton[:, first:last]).then_inc(norm_step, 1)
                    dve.wait_ge(norm_step, (B - 1 + part) * NEWTON_OPS + (k + 1))
                dve.scalar_tensor_tensor(out=shift[:, 1, first:last], in0=mean, scalar=-1.0, in1=result,
                                         op0=ALU.mult, op1=ALU.mult).then_inc(norm_ready, 1)

            def batch_extremes(n, loop):
                for k, op in enumerate((ALU.min, ALU.max)):
                    until(dve, extremes_step, 2 * n + k - 1, loop, 4)
                    dve.tensor_tensor(extremes[:, k, :], extremes[:, k, :], low[:, n % 2 * TILES:(n % 2 + 1) * TILES],
                                      op).then_inc(extremes_step, 1)

            def step(q, loop):
                if present(q + 1, loop):
                    mask_scores(q + 1, loop)
                normaliser(q, 0, loop)
                if present(q, loop):
                    invert(q, loop)
                if present(q + 1, loop):
                    join_lows(q + 1, loop)
                normaliser(q, 1, loop)
                if present(q, loop):
                    lower_pT(q, 0, loop)
                normaliser(q, 2, loop)
                if present(q, loop):
                    lower_pT(q, 1, loop)
                normaliser(q, 3, loop)
                if present(q + PREP, loop):
                    scale_x(q + PREP, loop)
                if q == -SCORES - 1:
                    angles()
                if q == -SCORES:
                    time_terms()
                normaliser(q, 4, loop)
                if present(q - 2, loop):
                    row_stats(q - 2, loop)
                normaliser(q, 5, loop)
                if present(q + SCORES, loop):
                    store_scores(q + SCORES, loop)
                normaliser(q, 6, loop)
                if present(q - 2, loop):
                    row_moments(q - 2, loop)
                if q % TILES == 4 and present(q - 4 - TILES, loop):
                    batch_extremes(q // TILES - 1, loop)

            def find_suspects():
                dve.wait_ge(extremes_step, 2 * B)
                dve.tensor_reduce(suspect[:, 0:1], extremes[:, 0, :], AX_X, ALU.min).then_inc(suspect_step, 1)
                dve.tensor_reduce(suspect[:, 1:2], extremes[:, 1, :], AX_X, ALU.max).then_inc(suspect_step, 1)
                dve.wait_ge(suspect_step, 2)
                dve.tensor_scalar(suspect[:, 0:1], suspect[:, 0:1], -1.0, None, ALU.mult).then_inc(suspect_step, 1)
                dve.wait_ge(suspect_step, 3)
                dve.tensor_tensor(suspect[:, 2:3], suspect[:, 0:1], suspect[:, 1:2], ALU.max).then_inc(suspect_step, 1)
                dve.wait_ge(suspect_step, 4)
                dve.tensor_scalar(suspect[:, 3:4], suspect[:, 2:3], SUSPECT, None, ALU.is_ge).then_inc(suspect_ready, 1)

            def general():
                with dve.Fori(0, B) as b:
                    with dve.Fori(0, TILES) as t:
                        g = b * TILES + t
                        dve.wait_ge(g_xT_copied, b * (DC * HALVES) + DC * HALVES)
                        for r in range(R):
                            for k in range(DC):
                                last = dve.tensor_scalar(g_ax[:, r, k, :], g_xT[:, k, bass.ds(t * P, P)], a_cols[:, k, r:r + 1],
                                                         None, ALU.mult)
                        last.then_inc(g_ax_ready, 1)
                        dve.memset(g_alpha, NEG).then_inc(g_cleared, 1)
                        dve.wait_ge(g_cleared, g + 1)
                        dve.wait_ge(g_adj_loaded, g * 16 + 16)
                        for r in range(R):
                            if r > 0:
                                dve.wait_ge(g_selected, g * R + r)
                            dve.tensor_scalar(g_is_rel, g_adj, float(r + 1), None, ALU.is_equal).then_inc(g_is_rel_ready, 1)
                            dve.wait_ge(g_biased_ready, g * R + (r + 1))
                            dve.scalar_tensor_tensor(out=g_leaky, in0=g_biased, scalar=SLOPE, in1=g_biased,
                                                     op0=ALU.mult, op1=ALU.max).then_inc(g_leaky_ready, 1)
                            dve.wait_ge(ident_ready, 1)
                            dve.wait_ge(g_leaky_ready, g * R + (r + 1))
                            dve.wait_ge(g_is_rel_ready, g * R + (r + 1))
                            dve.copy_predicated(g_alpha, g_is_rel, g_leaky).then_inc(g_selected, 1)
                        dve.wait_ge(g_selected, g * R + R)
                        dve.tensor_reduce(inv[:, 0:1], g_alpha, AX_X, ALU.max).then_inc(g_peak, 1)
                        dve.wait_ge(g_peak, g + 1)
                        dve.tensor_scalar(low[:, 0:1], inv[:, 0:1], -1.0, None, ALU.mult).then_inc(g_low_ready, 1)
                        dve.wait_ge(g_probs_ready, g + 1)
                        dve.reciprocal(inv[:, 1:2], sums[:, 0:1]).then_inc(g_inv_ready, 1)
                        dve.wait_ge(g_inv_ready, g + 1)
                        dve.wait_ge(g_o_ready, g + 1)
                        dve.scalar_tensor_tensor(out=g_y, in0=ps_o[:], scalar=inv[:, 1:2],
                                                 in1=g_x[:, bass.ds(t, 1), :].rearrange("p a d -> p (a d)"),
                                                 op0=ALU.mult, op1=ALU.add).then_inc(g_y_ready, 1)
                        dve.wait_ge(g_y_ready, g + 1)
                        dve.bn_stats(stats[:, 0, :], g_y).then_inc(g_stats_ready, 1)
                        dve.wait_ge(ident_ready, 1)
                        dve.wait_ge(g_stats_ready, g + 1)
                        dve.bn_aggr(moments[:, 0, 0, :], stats[:, 0, :]).then_inc(g_moments_ready, 1)
                        dve.wait_ge(g_moments_ready, g + 1)
                        for k in range(NEWTON_OPS):
                            newton_rsqrt(k, rstd[:, 0, 0:1], moments[:, 0, 0, 1:2], newton[:, 0:1]).then_inc(g_rstd_step, 1)
                            dve.wait_ge(g_rstd_step, g * NEWTON_OPS + (k + 1))
                        dve.tensor_scalar(g_out, g_y, moments[:, 0, 0, 0:1], rstd[:, 0, 0:1], ALU.subtract, ALU.mult).then_inc(g_normed, 1)
                        dve.wait_ge(g_stored, g * 16 + 16)

            parameters()
            steps(dve, step, -PREP, ALL)
            normaliser_of_last(0)
            step(ALL, None)
            batch_extremes(B - 1, None)
            find_suspects()
            step(ALL + 1, None)
            normaliser_of_last(1)
            dve.wait_ge(suspects_summed, 1)
            dve.tensor_copy(flag[:], ps_x[0:1, 0, 0:1]).then_inc(flag_ready, 1)
            dve.wait_ge(flag_ready, 1)
            with dve.If(dve.value_load(flag[0:1, 0:1]) != 0):
                for stored, stores in zip(out_stored, STORES):
                    dve.wait_ge(stored, 16 * stores)
                general()

        @block.tensor
        def _(pe):
            pe.wait_ge(ident_ready, 1)

            def transpose_probs(q, loop):
                until(pe, probs_ready, q + 1, loop, PAIR)
                for h in range(HALVES):
                    until(pe, pT_lo_ready, 2 * q - 1 + h, loop, 2 * PAIR)
                    for c in range(h * PER, (h + 1) * PER):
                        last = pe.transpose(ps_pT[:, c, :], probs[:, q % 2, c * P:(c + 1) * P], ident[:])
                    last.then_inc(pT_ready, 1)

            def transpose_scores(q, loop):
                t = q % TILES
                if t == TILES - 1:
                    return
                until(pe, group_stored, (q // TILES + 1) * GROUPS, loop, 2 * GROUPS)
                until(pe, low_ready, q, loop, PAIR)
                for c in range(t + 1, TILES):
                    last = pe.transpose(ps_sT[:, c * P:(c + 1) * P], scores[:, q // TILES % 2, triangle(c) + t, :], ident[:])
                last.then_inc(sT_ready, 1)

            def multiply_scores(s, loop):
                batch, half = s // TILES, s // TILES % 2
                for k, group in enumerate(SETS[s % TILES]):
                    n = batch * GROUPS + GROUPS_BEFORE[s % TILES] + k
                    row = max(row for row, _, _ in group)
                    until(pe, xT_lo_ready, batch * TILES + row + 1, loop, PAIR)
                    until(pe, ax_lo_ready, batch * TILES + row + 1, loop, PAIR)
                    until(pe, group_stored, n - 1, loop, 2 * GROUPS)
                    place = 0
                    for row, column, count in group:
                        width = max(count, 2) * P
                        target = ps_scores[:, n % 2, place * P:place * P + width]
                        columns = slice(column * P, column * P + width)
                        for d in range(DC):
                            for m, (left, right) in enumerate(((ax_hi, xT_hi), (ax_hi, xT_lo), (ax_lo, xT_hi))):
                                last = pe.matmul(target, left[:, row, d, :], right[:, half, d, columns],
                                                 start=(d == 0 and m == 0), stop=(d == DC - 1 and m == 2))
                        place += count
                    last.then_inc(group_multiplied, 1)

            def transpose_x(g, loop):
                until(pe, x_loaded[g % PAIR // 2], 16 * (g // PAIR + 1), loop, 16)
                until(pe, xT_lo_ready, g - 1 if loop is None and g < PREP else g, loop, PAIR)
                for d in range(DC):
                    last = pe.transpose(x_place(g, loop)[:, d, :], x_rows[:, g % PAIR, d * P:(d + 1) * P], ident[:])
                last.then_inc(xT_ready, 1)

            def attend(q, loop):
                half = q // TILES % 2
                until(pe, x_lo_ready, (q // TILES + 1) * TILES, loop, PAIR)
                until(pe, o_scaled, q, loop, PAIR)
                for c in range(TILES):
                    if c % PER == 0:
                        until(pe, pT_lo_ready, 2 * q + c // PER + 1, loop, 2 * PAIR)
                    for m, (left, right) in enumerate(((pT_hi, x_hi), (pT_hi, x_lo), (pT_lo, x_hi))):
                        last = pe.matmul(ps_o[:], left[:, q % 2, c, :], right[:, half, c, :],
                                         start=(c == 0 and m == 0), stop=(c == TILES - 1 and m == 2))
                last.then_inc(o_ready, 1)

            def step(q, loop):
                if present(q + 1, loop):
                    transpose_scores(q + 1, loop)
                if present(q, loop):
                    transpose_probs(q, loop)
                for g in blocks_at(q, loop):
                    transpose_x(g, loop)
                if present(q - 1, loop):
                    attend(q - 1, loop)
                if present(q + SCORES, loop):
                    multiply_scores(q + SCORES, loop)
                if q == -SCORES:
                    pe.wait_ge(time_terms_ready, 1)
                    pe.matmul(ps_pT[:, 0, 0:R], ones[0:T, :], phase[:, 3, :], start=True, stop=True).then_inc(c_summed, 1)

            def general():
                with pe.Fori(0, B) as b:
                    pe.wait_ge(g_x_loaded, b * 16 + 16)
                    for k in range(DC):
                        for h in range(HALVES):
                            if k + h > 0:
                                pe.wait_ge(g_xT_copied, b * (DC * HALVES) + (k * HALVES + h))
                            for c in range(h * PER, (h + 1) * PER):
                                last = pe.transpose(ps_pT[:, c, :], g_x[:, c, k * P:(k + 1) * P], ident[:])
                            last.then_inc(g_xT_ready, 1)
                    with pe.Fori(0, TILES) as t:
                        g = b * TILES + t
                        pe.wait_ge(g_ax_ready, g + 1)
                        for r in range(R):
                            if r > 0:
                                pe.wait_ge(g_biased_ready, g * R + r)
                            for h in range(HALVES):
                                for k in range(DC):
                                    last = pe.matmul(ps_sT[:, h * BANK:(h + 1) * BANK], g_ax[:, r, k, :],
                                                     g_xT[:, k, h * BANK:(h + 1) * BANK], start=(k == 0), stop=(k == DC - 1))
                            last.then_inc(g_scores_ready, 1)
                        pe.wait_ge(g_probs_ready, g + 1)
                        for c in range(TILES):
                            last = pe.transpose(ps_pT[:, c, :], g_alpha[:, c * P:(c + 1) * P], ident[:])
                        last.then_inc(g_pT_ready, 1)
                        pe.wait_ge(g_pT_copied, g + 1)
                        for c in range(TILES):
                            last = pe.matmul(ps_o[:], g_pT[:, c, :], g_x[:, c, :], start=(c == 0), stop=(c == TILES - 1))
                        last.then_inc(g_o_ready, 1)

            steps(pe, step, -PREP, ALL + 1)
            pe.wait_ge(suspect_ready, 1)
            pe.matmul(ps_x[0:1, 0, 0:1], suspect[:, 3:4], ones[:, 0:1], start=True, stop=True).then_inc(suspects_summed, 1)
            pe.wait_ge(flag_ready, 1)
            with pe.If(pe.value_load(flag[0:1, 0:1]) != 0):
                general()


_INS = ["x", "adj", "L0_gnn_a_rel", "L0_gnn_t_rel", "L0_gnn_time_w"]


def kernel(**inputs):
    import numpy as _np
    import concourse.bacc as _bacc
    from concourse import mybir as _mybir
    from concourse.bass_utils import run_bass_kernel_spmd as _run

    nc = _bacc.Bacc("TRN2", target_bir_lowering=False, num_devices=1)
    arrays, args = {}, []
    for name in _INS:
        a = _np.ascontiguousarray(inputs[name])
        arrays[f"in_{name}_dram"] = a
        args.append(nc.dram_tensor(f"in_{name}_dram", a.shape, _mybir.dt.from_np(a.dtype), kind="ExternalInput").ap())
    shape = tuple(inputs["x"].shape)
    args.append(nc.dram_tensor("out_0_dram", shape, _mybir.dt.float32, kind="ExternalOutput").ap())
    relation_attention(nc, *args)
    r = _run(nc, [arrays], core_ids=[0])
    return r.results[0]["out_0_dram"]
```
